# Optimizing a Trainium2 kernel written in Bass

```python
import numpy as np
import jax
import jax.numpy as jnp

def _softmax(x, axis=-1):
    return jax.nn.softmax(x, axis=axis)

def _gelu(x):
    return jax.nn.gelu(x, approximate=True)

def _silu(x):
    return jax.nn.silu(x)

def _sigmoid(x):
    return jax.nn.sigmoid(x)

def _layernorm(x, axis=-1, eps=1e-05):
    m = jnp.mean(x, axis=axis, keepdims=True)
    v = jnp.var(x, axis=axis, keepdims=True)
    return (x - m) / jnp.sqrt(v + eps)

def _scatter_add(tgt, idx, src, axis=0):
    return tgt.at[idx].add(src)

def _segment_sum(src, seg, n):
    return jax.ops.segment_sum(src, seg, n)
kernel_name = 'mk_macaron_d1_jaxref_r2_a0cfcf'

def setup_inputs(seed: int=0):
    np.random.seed(seed)
    _w = jnp.asarray

    def _L0_attn_setup():
        import jax, jax.numpy as jnp
        import numpy as np
        import math
        B, T, E = (1, 1024, 512)
        H = 16
        D = E // H
        L = 64
        key = jax.random.key(seed)
        ks = jax.random.split(key, 7)
        s = lambda fan: 1.0 / math.sqrt(fan)
        return {'hidden_states': jax.random.normal(ks[0], (B, T, E), dtype=jnp.float32), 'Wq': jax.random.normal(ks[1], (E, E), dtype=jnp.float32) * s(E), 'Wk_down': jax.random.normal(ks[2], (L, E), dtype=jnp.float32) * s(E), 'Wv_down': jax.random.normal(ks[3], (L, E), dtype=jnp.float32) * s(E), 'q_to_latent': jax.random.normal(ks[4], (H, D, L), dtype=jnp.float32) * s(D), 'v_up': jax.random.normal(ks[5], (H, L, D), dtype=jnp.float32) * s(L), 'Wout': jax.random.normal(ks[6], (E, E), dtype=jnp.float32) * s(E)}
    _L0_attn_in = _L0_attn_setup()

    def _L0_ffn_setup():
        import jax, jax.numpy as jnp
        import numpy as np
        CAPACITY_RATIO = 0.75
        key = jax.random.key(seed)
        k1, k2, k3 = jax.random.split(key, 3)
        B, L, D = (4, 4096, 512)
        x = jax.random.normal(k1, (B, L, D), dtype=jnp.float32)
        w_router = jax.random.normal(k2, (D,), dtype=jnp.float32) * 0.02
        w_block = jax.random.normal(k3, (D, D), dtype=jnp.float32) * 0.02
        return {'x': x, 'w_router': w_router, 'w_block': w_block}
    _L0_ffn_in = _L0_ffn_setup()
    _d = {'L0_attn_hidden_states': _L0_attn_in['hidden_states'], 'L0_attn_Wq': _L0_attn_in['Wq'], 'L0_attn_Wk_down': _L0_attn_in['Wk_down'], 'L0_attn_Wv_down': _L0_attn_in['Wv_down'], 'L0_attn_q_to_latent': _L0_attn_in['q_to_latent'], 'L0_attn_v_up': _L0_attn_in['v_up'], 'L0_attn_Wout': _L0_attn_in['Wout'], 'L0_ffn_w_router': _L0_ffn_in['w_router'], 'L0_ffn_w_block': _L0_ffn_in['w_block']}
    _x0 = _d['L0_attn_hidden_states']
    _d['L0_attn_hidden_states'] = jax.random.normal(jax.random.fold_in(jax.random.key(seed), 1), (8, 1024, 512), dtype=_x0.dtype)
    del _x0
    return _d

def reference(L0_attn_hidden_states, L0_attn_Wq, L0_attn_Wk_down, L0_attn_Wv_down, L0_attn_q_to_latent, L0_attn_v_up, L0_attn_Wout, L0_ffn_w_router, L0_ffn_w_block):

    def _L0_attn_ref(hidden_states, Wq, Wk_down, Wv_down, q_to_latent, v_up, Wout):
        import jax, jax.numpy as jnp
        import numpy as np
        import math
        B, T, E = (1, 1024, 512)
        H = 16
        D = E // H
        L = 64
        'RA_MLA_Attention forward (default config: coupling_scale=0 so the RA\n            reciprocal-band branch is inactive; no cache, no RoPE, dropout=0).'
        b, t, e = hidden_states.shape
        h, d, l = q_to_latent.shape
        Q = (hidden_states @ Wq.T).reshape(b, t, h, d)
        latent_k = hidden_states @ Wk_down.T
        latent_v = hidden_states @ Wv_down.T
        q_lat = jnp.einsum('bthd,hdl->bthl', Q, q_to_latent)
        logits = jnp.einsum('bthl,bsl->bhts', q_lat, latent_k) / math.sqrt(l)
        causal = jnp.tril(jnp.ones((t, t), dtype=bool))
        logits = jnp.where(causal[None, None], logits, jnp.float32(-1e+30))
        attn = jax.nn.softmax(logits, axis=-1)
        ctx_lat = jnp.einsum('bhts,bsl->bhtl', attn, latent_v)
        heads = jnp.einsum('bhtl,hld->bthd', ctx_lat, v_up)
        out = heads.reshape(b, t, h * d) @ Wout.T
        return out

    def _L0_ffn_ref(x, w_router, w_block):
        import jax, jax.numpy as jnp
        import numpy as np
        CAPACITY_RATIO = 0.75
        B, L, D = x.shape
        k = max(1, int(L * CAPACITY_RATIO))
        scores = jnp.einsum('bld,d->bl', x, w_router)
        _, top_idx = jax.lax.top_k(scores, k)
        selected = jnp.take_along_axis(x, top_idx[:, :, None], axis=1)
        processed = jax.nn.gelu(jnp.einsum('bkd,de->bke', selected, w_block))
        batch_idx = jnp.arange(B)[:, None]
        out = x.at[batch_idx, top_idx].set(processed)
        return out
    x = L0_attn_hidden_states
    x = x + 0.5 * _L0_ffn_ref(_layernorm(x, axis=-1), L0_ffn_w_router, L0_ffn_w_block)
    x = x + _L0_attn_ref(_layernorm(x, axis=-1), L0_attn_Wq, L0_attn_Wk_down, L0_attn_Wv_down, L0_attn_q_to_latent, L0_attn_v_up, L0_attn_Wout)
    x = x + 0.5 * _L0_ffn_ref(_layernorm(x, axis=-1), L0_ffn_w_router, L0_ffn_w_block)
    return x

_drawn_inputs = setup_inputs


def setup_inputs(seed=0):
    import zlib

    import numpy as np

    out = dict(_drawn_inputs(seed))
    spreads = {}
    factors = {}
    for name, (base, spread) in spreads.items():
        noise = np.random.default_rng([zlib.crc32(name.encode()), seed]).standard_normal(out[name].shape)
        drawn = base * np.exp(spread * noise) if base else spread * noise
        out[name] = jnp.asarray(drawn.astype(out[name].dtype))
    for name, factor in factors.items():
        out[name] = (out[name] * factor).astype(out[name].dtype)
    return out
```

```python
from contextlib import ExitStack

import concourse.bass as bass
from concourse import mybir

F32 = mybir.dt.float32
F32R = mybir.dt.float32r
BF16 = mybir.dt.bfloat16
ACT = mybir.ActivationFunctionType
ALU = mybir.AluOpType
AX_X = mybir.AxisListType.X

P = 128
BANK = 512
EPS = 1e-5
CAPACITY = 0.75
FAR = -1e30
LEAD = 19
SLOTS = 6


def macaron(nc, x, w_q, w_lat, w_qk, w_vu, w_out, w_router, w_block, scratch_q, scratch_o, out):
    B, T, E = x.shape
    L, HD = w_qk.shape
    DH = 32
    NT = T // P
    NK = E // P
    NQ = HD // P
    HQ = P // DH
    NC = T // BANK
    TC = NT // NC
    KEEP = max(1, int(T * CAPACITY))
    SCALE = float(L) ** -0.5
    assert 2 * L == P and HD == E and (NT, NK, NQ, NC, TC) == (8, 4, 4, 2, 4)
    ROWS = 3 * DH
    STACK = 16 * 3
    USES = HQ * 2 * (1 + 2)
    RAW = 16 * (4 + 3 * NK)
    CONSTS = 7

    CHUNKS = tuple(reversed(range(NC)))
    maxima = []
    for g in range(NQ):
        maxima += [("MX", g, i, (h,)) for i in range(TC, NT) for h in range(HQ)] + [("XT", g, 1)]
        maxima += [("MX", g, i, (2 * p, 2 * p + 1)) for i in range(TC) for p in range(2)] + [("XT", g, 0)]
    uses = [(g, c, jp, h) for g in range(NQ) for c in CHUNKS for jp in range(2 * (c + 1)) for h in range(HQ)]
    steps = [(g, c, jp) for g in range(NQ) for c in CHUNKS for jp in range(2 * (c + 1))]
    fill = [("V", 0), ("V", 1), ("V", 2), ("V", 3), ("K", 1, 1), ("KD", 1, 1), ("Q", 2, 1), ("QST", 1, 1), ("QD", 1, 1),
            ("V", 4), ("V", 5), ("K", 1, 0), ("KD", 1, 0), ("Q", 2, 0), ("QST", 1, 0), ("QD", 1, 0),
            ("V", 6), ("V", 7), ("Q", 3, 1), ("Q", 3, 0)]
    sched = [("Q", 0, 1), ("Q", 0, 0), ("K", 0, 1), ("KD", 0, 1), ("QST", 0, 1), ("QD", 0, 1), ("Q", 1, 1),
             ("K", 0, 0), ("KD", 0, 0), ("QST", 0, 0), ("QD", 0, 0), ("Q", 1, 0)]
    at = 0
    for u in range(len(uses)):
        g, r = u // USES, u % USES
        if g + 2 < NQ:
            sched += {USES - 6: [("K", g + 2, 1), ("KD", g + 2, 1)], USES - 4: [("QST", g + 2, 1), ("QD", g + 2, 1)],
                      USES - 2: [("K", g + 2, 0)]}.get(r, [])
        if 1 <= g < NQ - 1:
            sched += {0: [("KD", g + 1, 0)], 3: [("QST", g + 1, 0), ("QD", g + 1, 0)]}.get(r, [])
        upto = min(len(maxima), -(-(u + LEAD) * len(maxima) // len(uses)))
        while at < upto:
            sched.append(maxima[at])
            if u == 0 and fill:
                sched.append(fill.pop(0))
            at += 1
        if u == 0:
            sched += fill
        sched.append(("S", u))
        if u % HQ == 1 and u > HQ:
            sched.append(("PV", u // HQ - 1))
        if u % HQ == 3 and u > HQ:
            sched.append(("DEN", u // HQ - 1))
    last = len(steps) - 1
    sched += [("PV", last), ("DEN", last)]
    uses_of_m = [e for e in sched if e[0] in ("K", "MX", "XT")]
    m_index = {e: n + 1 for n, e in enumerate(uses_of_m)}
    N_M = len(uses_of_m)
    q_order = [e[1:] for e in sched if e[0] == "Q"]

    def order_of(g, c):
        return NC * g + CHUNKS.index(c) + 1

    def width(c, j):
        return BANK - max(0, P * j - BANK * c)

    def diagonal(u):
        g, c, jp, h = uses[u]
        return 2 * jp >= TC * c

    masks_upto = [0]
    for u in range(len(uses)):
        masks_upto.append(masks_upto[-1] + diagonal(u))
    sums_upto = [0]
    for u in range(len(uses)):
        sums_upto.append(sums_upto[-1] + (2 if diagonal(u) else 1))

    with ExitStack() as ctx:
        def sb(name, shape, dt=F32, stack=ctx):
            return stack.enter_context(nc.sbuf_tensor(name, shape, dt))

        def sem(name):
            return ctx.enter_context(nc.semaphore(name))

        x1 = sb("x1", [P, NT, E])
        wb_h, wb_l = sb("wb_h", [P, NK, E], F32R), sb("wb_l", [P, NK, E], F32R)
        w2_h, w2_l = sb("w2_h", [P, NK, E], F32R), sb("w2_l", [P, NK, E], F32R)
        wlat_h, wlat_l = sb("wlat_h", [P, NK, P], F32R), sb("wlat_l", [P, NK, P], F32R)
        wkv_h, wkv_l = sb("wkv_h", [P, HD], F32R), sb("wkv_l", [P, HD], F32R)
        wr_h, wr_l = sb("wr_h", [P, NK], F32R), sb("wr_l", [P, NK], F32R)
        ident = sb("ident", [P, P])
        ident_b = sb("ident_b", [P, P], BF16)
        mask_b = sb("mask_b", [P, P], BF16)
        ones = sb("ones", [P, DH])
        earlier = sb("earlier", [P, T], BF16)
        half = sb("half", [P, NT])
        stats = sb("stats", [P, NT, 6])
        mv = sb("mv", [P, NT, 2])
        var = sb("var", [P, NT])
        rstd = sb("rstd", [P, NT])
        nmr = sb("nmr", [P, NT])
        scol = sb("scol", [P, NT])
        n_gt = sb("n_gt", [P, NT])
        n_eq = sb("n_eq", [P, NT])
        sel = sb("sel", [P, NT])
        rest = sb("rest", [P, NT])
        gain = sb("gain", [P, NT])
        shift = sb("shift", [P, NT])
        mx = sb("mx", [P, NC, HQ, TC])
        mxt = sb("mxt", [HQ * TC, P], F32R)
        acc_sb = sb("acc_sb", [P, BANK])
        ht = sb("ht", [P, NQ, T])
        lat_h, lat_l = sb("lat_h", [P, T], F32R), sb("lat_l", [P, T], F32R)
        with ExitStack() as turn:
            nt_h, nt_l = sb("nt_h", [P, NK, T], F32R, turn), sb("nt_l", [P, NK, T], F32R, turn)
        pr = sb("pr", [P, SLOTS, 2 * BANK])
        dsum = sb("dsum", [P, HQ, BANK])
        with ExitStack() as turn:
            act_out = sb("act_out", [P, NT, E], F32, turn)
        v_sb = sb("v_sb", [P, NT, HD])
        with ExitStack() as turn:
            norm = sb("norm", [P, 4, E], F32, turn)
        kst_h, kst_l = sb("kst_h", [P, BANK], F32R), sb("kst_l", [P, BANK], F32R)
        qst_h, qst_l = sb("qst_h", [P, BANK], F32R), sb("qst_l", [P, BANK], F32R)
        ks = sb("ks", [P, 2, NC, HQ, BANK], F32R)
        with ExitStack() as turn:
            xin = sb("xin", [P, NT, E], F32, turn)
            srow = sb("srow", [P, T], F32, turn)
            junk = sb("junk", [P, T], BF16, turn)
        qs = sb("qs", [P, 2, NC, HQ, BANK], F32R)

        wide = ht[:].rearrange("p g t -> p (g t)")
        flat = [t[:].rearrange("p k n -> p (k n)") for t in (wb_h, wb_l, w2_h, w2_l, wlat_h, wlat_l)]
        raw_block = x1[:, 0:NK, :].rearrange("p k n -> p (k n)")
        raw_out = x1[:, NK:2 * NK, :].rearrange("p k n -> p (k n)")
        weight_parts_h = [(flat[0], raw_block), (flat[2], raw_out)]
        weight_parts_l = [flat[1], flat[3]]
        weight_parts_h += [(flat[4], wide[:, 2 * T:2 * T + E]), (wkv_h[:], wide[:, 2 * T + E:3 * T]),
                           (wr_h[:], wide[:, 3 * T:3 * T + NK]), (flat[2], wide[:, 0:2 * T])]
        weight_parts_l += [flat[5], wkv_l[:], wr_l[:], flat[3]]

        def ps(name, banks):
            return ctx.enter_context(nc.psum_tensor(name, [P, banks * BANK], F32))
        score = [ps("score0", 2), ps("score1", 2)]
        mxp = ps("mxp", 2)
        acc, den = ps("acc", 1), ps("den", 1)
        turned = [score[0][:, 0:BANK], score[0][:, BANK:2 * BANK]]
        prod = [score[1][:, 0:BANK], score[1][:, BANK:2 * BANK]]
        vbank = [acc, den]

        raw_in, split, scr_out = sem("raw_in"), sem("split"), sem("scr_out")
        pool_init, consts = sem("pool_init"), sem("consts")
        loop_sems = []

        def lsem(name):
            s = sem(name)
            loop_sems.append(s)
            return s
        x_in, x_out, w2_in = [lsem(f"x_in{c}") for c in range(NC)], lsem("x_out"), lsem("w2_in")
        var_ready, rstd_ready, nmr_ready = lsem("var_ready"), lsem("rstd_ready"), lsem("nmr_ready")
        norm_ready, turn_done = lsem("norm_ready"), lsem("turn_done")
        nth_ready, ntl_ready = lsem("nth_ready"), lsem("ntl_ready")
        sc_done, srow_ready, scol_done, scol_ready = lsem("sc_done"), lsem("srow_ready"), lsem("scol_done"), lsem("scol_ready")
        z_done, gelu_ready, x1_ready = lsem("z_done"), lsem("gelu_ready"), lsem("x1_ready")
        lat_done, lath_ready, latl_ready = lsem("lat_done"), lsem("lath_ready"), lsem("latl_ready")
        q_done, q_ready, v_done, v_ready = lsem("q_done"), lsem("q_ready"), lsem("v_done"), lsem("v_ready")
        kh_ready, qh_ready, ql_ready = lsem("kh_ready"), lsem("qh_ready"), lsem("ql_ready")
        k_stack, q_stack, m_stack = lsem("k_stack"), lsem("q_stack"), lsem("m_stack")
        m_done, m_free = lsem("m_done"), lsem("m_free")
        s_done, exp_ready, mask_ready, sum_ready = lsem("s_done"), lsem("exp_ready"), lsem("mask_ready"), lsem("sum_ready")
        pv_done, den_done, bank_free, heads_ready = lsem("pv_done"), lsem("den_done"), lsem("bank_free"), lsem("heads_ready")
        oh_ready, ol_ready, o_done = lsem("oh_ready"), lsem("ol_ready"), lsem("o_done")
        dve_step, arrived = lsem("dve_step"), lsem("arrived")
        go, passed = sem("go"), sem("passed")
        first, final = loop_sems[0].num, loop_sems[-1].num
        assert [s.num for s in loop_sems] == list(range(first, final + 1)) and passed.num == go.num + 1

        block = ctx.enter_context(nc.Block())

        def end_of_sequence(eng):
            eng.sem_inc(arrived, 1)
            eng.wait_ge(go, 1)
            eng.sem_inc(passed, 1)

        @block.sync
        def _(sp):
            sp.dma_start(x1[:, 0:NK, :], w_block.rearrange("(k p) n -> p k n", p=P)).then_inc(raw_in, 16)
            sp.dma_start(x1[:, NK:2 * NK, :], w_out.rearrange("(k p) n -> p k n", p=P)).then_inc(raw_in, 16)
            for k in range(NK):
                sp.dma_start(ht[:, k // 2, (k % 2) * E:(k % 2 + 1) * E], w_q[k * P:(k + 1) * P, :]).then_inc(raw_in, 16)
                sp.dma_start(ht[:, 2, k * P:(k + 1) * P], w_lat[k * P:(k + 1) * P, :]).then_inc(raw_in, 16)
                sp.dma_start(ht[:, 3, k:k + 1], w_router[k * P:(k + 1) * P].rearrange("(p o) -> p o", o=1)).then_inc(raw_in, 16)
            sp.dma_start(ht[0:L, 2, E:2 * E], w_qk).then_inc(raw_in, 16)
            sp.dma_start(ht[L:P, 2, E:2 * E], w_vu).then_inc(raw_in, 16)
            sp.wait_ge(split, 4)
            sp.dma_start(scratch_o[0], w2_h[:].bitcast(F32)).then_inc(scr_out, 16)
            sp.dma_start(scratch_o[1], w2_l[:].bitcast(F32)).then_inc(scr_out, 16)
            sp.wait_ge(split, 12)
            sp.dma_start(scratch_q[0], w2_h[:].bitcast(F32)).then_inc(scr_out, 16)
            sp.dma_start(scratch_q[1], w2_l[:].bitcast(F32)).then_inc(scr_out, 16)
            sp.wait_ge(scr_out, 64)

            with sp.Fori(0, B) as b:
                for c in range(NC):
                    sp.dma_start(xin[:, TC * c:TC * (c + 1), :],
                                 x[bass.ds(b, 1), c * BANK:(c + 1) * BANK, :].rearrange("o (i p) e -> p (o i) e", p=P)
                                 ).then_inc(x_in[c], 16)

                def stack(dst, order, signal):
                    for r, src in enumerate(order):
                        sp.dma_start(dst[r * DH:(r + 1) * DH, :, :].bitcast(F32), src[:].bitcast(F32)).then_inc(signal, 16)

                sp.wait_ge(x1_ready, NT)
                for e in sched:
                    if e[0] in ("KD", "QD"):
                        g, c = e[1:]
                        if g >= 2:
                            sp.wait_ge(s_done, USES * (g - 2) + (USES if c == 0 else 4 * HQ))
                        if e[0] == "KD":
                            sp.wait_ge(m_free, m_index[("K", g, c)])
                            stack(ks[:, g % 2, c], (kst_h, kst_h, kst_l), k_stack)
                        else:
                            sp.wait_ge(ql_ready, order_of(g, c))
                            stack(qs[:, g % 2, c], (qst_h, qst_l, qst_h), q_stack)
                    elif e[0] == "XT":
                        g, c = e[1:]
                        sp.wait_ge(m_free, m_index[e])
                        sp.dma_start(qs[ROWS:ROWS + 1, g % 2, c].rearrange("p h t -> p (h t)").bitcast(F32),
                                     mxt[:].bitcast(F32)).then_inc(m_stack, 16)
                        if (g, c) == (0, 1):
                            sp.wait_ge(q_done, NQ * NC)
                            sp.dma_start(w2_h[:].bitcast(F32), scratch_o[0]).then_inc(w2_in, 16)
                            sp.dma_start(w2_l[:].bitcast(F32), scratch_o[1]).then_inc(w2_in, 16)
                sp.wait_ge(o_done, NT)
                sp.wait_ge(w2_in, 32)
                sp.dma_start(w2_h[:].bitcast(F32), scratch_q[0]).then_inc(w2_in, 16)
                sp.dma_start(w2_l[:].bitcast(F32), scratch_q[1]).then_inc(w2_in, 16)
                for c in range(NC):
                    sp.wait_ge(x1_ready, 2 * NT + TC * (c + 1))
                    sp.dma_start(out[bass.ds(b, 1), c * BANK:(c + 1) * BANK, :].rearrange("o (i p) e -> p (o i) e", p=P),
                                 x1[:, TC * c:TC * (c + 1), :]).then_inc(x_out, 16)
                sp.wait_ge(x_out, 16 * NC)
                sp.wait_ge(w2_in, 64)
                sp.wait_ge(arrived, 4)
                sp.sem_clear(range(first, final + 1))
                sp.sem_inc(go, 1)
                sp.wait_ge(passed, 4)
                sp.sem_clear(range(go.num, passed.num + 1))

        @block.gpsimd
        def _(pool):
            nc.gpsimd.memset(ident[:], 0.0).then_inc(pool_init, 1)
            nc.gpsimd.memset(ident_b[:], 0.0).then_inc(pool_init, 1)
            nc.gpsimd.memset(mask_b[:], 0.0).then_inc(pool_init, 1)
            nc.gpsimd.memset(earlier[:], 1.0).then_inc(pool_init, 1)
            nc.gpsimd.memset(ones[:], 1.0).then_inc(consts, 1)
            nc.gpsimd.memset(half[:], -0.5).then_inc(consts, 1)
            pool.wait_ge(pool_init, 4)
            for m in (ident, ident_b):
                nc.gpsimd.affine_select(out=m[:], in_=m[:], compare_op=ALU.not_equal, fill=1.0, base=0,
                                        pattern=[[-1, P]], channel_multiplier=1).then_inc(consts, 1)
            nc.gpsimd.affine_select(out=mask_b[:], in_=mask_b[:], compare_op=ALU.is_ge, fill=FAR, base=0,
                                    pattern=[[-1, P]], channel_multiplier=1).then_inc(consts, 1)
            nc.gpsimd.affine_select(out=earlier[:], in_=earlier[:], compare_op=ALU.is_gt, fill=0.0, base=T - P,
                                    pattern=[[-1, T]], channel_multiplier=1).then_inc(consts, 1)
            pool.wait_ge(consts, CONSTS)

            with pool.Fori(0, B):
                def rstd_of(s):
                    for c in range(NC):
                        k = slice(TC * c, TC * (c + 1))
                        pool.wait_ge(var_ready, NC * s + c + 1)
                        nc.gpsimd.tensor_tensor(rstd[:, k], var[:, k], half[:, k], ALU.pow).then_inc(rstd_ready, 1)

                rstd_of(0)
                rstd_of(1)
                for e in sched:
                    if e[0] == "QST":
                        g, c = e[1:]
                        pool.wait_ge(qh_ready, order_of(g, c))
                        nc.gpsimd.tensor_tensor(qst_l[:], ht[:, g, c * BANK:(c + 1) * BANK], qst_h[:].bitcast(F32),
                                                ALU.subtract).then_inc(ql_ready, 1)
                    elif e[0] == "S":
                        u = e[1]
                        g, c, jp, h = uses[u]
                        w0, w1 = width(c, 2 * jp), width(c, 2 * jp + 1)
                        slot = pr[:, u % SLOTS, :]
                        pool.wait_ge(exp_ready, u + 1)
                        if u >= HQ:
                            pool.wait_ge(den_done, u // HQ)
                        if diagonal(u):
                            tri = slot[:, 0:2 * w0].rearrange("p (a b) -> p a b", a=2)[:, :, 0:P]
                            nc.gpsimd.affine_select(out=tri, in_=tri, compare_op=ALU.is_ge, fill=0.0, base=0,
                                                    pattern=[[0, 2], [1, P]], channel_multiplier=-1
                                                    ).then_inc(mask_ready, 1)
                            pool.wait_ge(mask_ready, masks_upto[u + 1])
                            nc.gpsimd.tensor_copy(dsum[:, h, 0:P], slot[:, 0:P]).then_inc(sum_ready, 1)
                        nc.gpsimd.tensor_tensor(dsum[:, h, w0 - w1:w0], slot[:, w0 - w1:w0], slot[:, w0:w0 + w1], ALU.add
                                                ).then_inc(sum_ready, 1)
                rstd_of(2)
                end_of_sequence(pool)

        @block.scalar
        def _(act):
            act.wait_ge(raw_in, RAW)
            for n, (dst, raw) in enumerate(weight_parts_h):
                if n == 5:
                    act.wait_ge(scr_out, 32)
                nc.scalar.activation(dst, raw, ACT.Copy).then_inc(split, 1)
                act.wait_ge(split, 2 * n + 2)
            act.wait_ge(consts, CONSTS)

            with act.Fori(0, B):
                def normalise(s, tiles):
                    for i in tiles:
                        n = NT * s + i
                        src = xin if s == 0 else x1
                        act.wait_ge(nmr_ready, NC * s + i // TC + 1)
                        if n >= 4:
                            act.wait_ge(turn_done, n - 3)
                        if s == 2 and i == 0:
                            act.wait_ge(q_stack, STACK * NQ * NC)
                            act.wait_ge(k_stack, STACK * NQ * NC)
                        nc.scalar.activation(norm[:, i % 4, :], src[:, i, :], ACT.Identity, bias=nmr[:, i:i + 1],
                                             scale=rstd[:, i:i + 1]).then_inc(norm_ready, 1)

                def turned_high(s, tiles):
                    for i in tiles:
                        n = NT * s + i
                        act.wait_ge(turn_done, n + 1)
                        if s == 1:
                            act.wait_ge(z_done, i + 1)
                        if s == 2:
                            act.wait_ge(o_done, i + 1)
                        nc.scalar.activation(nt_h[:, :, P * i:P * (i + 1)],
                                             turned[i % 2].rearrange("p (k t) -> p k t", k=NK), ACT.Copy
                                             ).then_inc(nth_ready, 1)

                def score_row(f, c):
                    act.wait_ge(sc_done, NC * f + c + 1)
                    nc.scalar.activation(srow[:, c * BANK:(c + 1) * BANK], mxp[:, c * BANK:(c + 1) * BANK], ACT.Copy
                                         ).then_inc(srow_ready, 1)

                def gelu(f, tiles):
                    for i in tiles:
                        act.wait_ge(z_done, NT * f + i + 1)
                        nc.scalar.activation(act_out[:, i, :], prod[i % 2], ACT.Gelu_apprx_tanh).then_inc(gelu_ready, 1)

                def first_half(s):
                    for i in range(TC):
                        turned_high(s, [i])
                        normalise(s, [TC + i])

                normalise(0, range(TC))
                first_half(0)
                score_row(0, 0)
                turned_high(0, range(TC, NT))
                score_row(0, 1)
                gelu(0, range(6))
                normalise(1, range(TC))
                gelu(0, range(6, NT))
                first_half(1)
                for c in range(NC):
                    if c == 1:
                        turned_high(1, range(TC, NT))
                    act.wait_ge(lat_done, c + 1)
                    nc.scalar.activation(lat_h[:, c * BANK:(c + 1) * BANK], mxp[:, c * BANK:(c + 1) * BANK], ACT.Copy
                                         ).then_inc(lath_ready, 1)
                for e in sched:
                    if e[0] == "Q":
                        g, c = e[1:]
                        n = q_order.index((g, c))
                        act.wait_ge(q_done, n + 1)
                        nc.scalar.activation(ht[:, g, c * BANK:(c + 1) * BANK], prod[n % 2], ACT.Copy).then_inc(q_ready, 1)
                    elif e[0] == "K":
                        g, c = e[1:]
                        act.wait_ge(m_done, m_index[e])
                        if order_of(g, c) > 1:
                            act.wait_ge(k_stack, STACK * (order_of(g, c) - 1))
                        nc.scalar.activation(kst_h[:], mxp[:, 0:BANK], ACT.Copy).then_inc(kh_ready, 1)
                    elif e[0] == "QST":
                        g, c = e[1:]
                        act.wait_ge(q_ready, q_order.index((g, c)) + 1)
                        if order_of(g, c) > 1:
                            act.wait_ge(q_stack, STACK * (order_of(g, c) - 1))
                        nc.scalar.activation(qst_h[:], ht[:, g, c * BANK:(c + 1) * BANK], ACT.Copy).then_inc(qh_ready, 1)
                    elif e[0] == "S":
                        u = e[1]
                        g, c, jp, h = uses[u]
                        w0, w1 = width(c, 2 * jp), width(c, 2 * jp + 1)
                        if u == 0:
                            act.wait_ge(q_done, NQ * NC)
                        act.wait_ge(s_done, u + 1)
                        if u >= SLOTS:
                            act.wait_ge(pv_done, (u - SLOTS) // HQ + 1)
                            act.wait_ge(sum_ready, sums_upto[u - SLOTS + 1])
                        nc.scalar.activation(pr[:, u % SLOTS, 0:w0 + w1], score[u % 2][:, BANK - w0:BANK + w1], ACT.Exp,
                                             scale=SCALE).then_inc(exp_ready, 1)
                act.wait_ge(heads_ready, NQ * NC)
                for c in range(NC):
                    for g in range(NQ):
                        nc.scalar.activation(nt_h[:, g, c * BANK:(c + 1) * BANK], ht[:, g, c * BANK:(c + 1) * BANK],
                                             ACT.Copy).then_inc(oh_ready, 1)
                normalise(2, range(TC))
                first_half(2)
                act.wait_ge(s_done, USES * NQ)
                score_row(1, 0)
                turned_high(2, range(TC, NT))
                score_row(1, 1)
                act.wait_ge(pv_done, len(steps))
                gelu(1, range(NT))
                end_of_sequence(act)

        @block.tensor
        def _(pe):
            pe.wait_ge(consts, CONSTS)
            pe.wait_ge(split, 2 * len(weight_parts_h))

            def passes(o, a, b, n, a_cols, b_cols, rows=slice(0, P)):
                terms = [(a[0], b[0]), (a[0], b[1]), (a[1], b[0])]
                for k in range(n):
                    for t, (lhs, rhs) in enumerate(terms):
                        m = pe.matmul(o, a_cols(lhs, k), b_cols(rhs, k), start=(k == 0 and t == 0),
                                      stop=(k == n - 1 and t == 2))
                return m

            with pe.Fori(0, B):
                nt = (nt_h, nt_l)

                def turn_tiles(s, tiles):
                    for i in tiles:
                        n = NT * s + i
                        pe.wait_ge(norm_ready, n + 1)
                        if s == 2 and i < 2:
                            pe.wait_ge(exp_ready, USES * NQ)
                        elif n >= 2:
                            pe.wait_ge(ntl_ready, n - 1)
                        for k in range(NK):
                            m = pe.transpose(turned[i % 2][:, k * P:(k + 1) * P], norm[:, i % 4, k * P:(k + 1) * P], ident[:])
                        m.then_inc(turn_done, 1)

                def scores(f, c):
                    pe.wait_ge(ntl_ready, NT * 2 * f + TC * (c + 1))
                    if f == 1:
                        pe.wait_ge(m_free, N_M)
                    passes(mxp[:, c * BANK:(c + 1) * BANK], (wr_h, wr_l), nt, NK,
                           lambda w, k: w[:, k:k + 1].broadcast_to([P, P]),
                           lambda t, k: t[:, k, c * BANK:(c + 1) * BANK]).then_inc(sc_done, 1)

                def ffn(f):
                    pe.wait_ge(srow_ready, NC * (f + 1))
                    if f == 1:
                        pe.wait_ge(heads_ready, NQ * NC)
                    for i in range(NT):
                        m = pe.matmul(acc[:, i:i + 1], srow[0:1, P * i:P * (i + 1)], ident[0:1, 0:1], start=True, stop=True,
                                      is_transpose=True)
                    m.then_inc(scol_done, 1)
                    for i in range(NT):
                        if i >= 2:
                            pe.wait_ge(gelu_ready, NT * f + i - 1)
                        elif f == 1:
                            pe.wait_ge(x1_ready, 2 * NT)
                        passes(prod[i % 2], nt, (wb_h, wb_l), NK, lambda t, k: t[:, k, P * i:P * (i + 1)],
                               lambda w, k: w[:, k, :]).then_inc(z_done, 1)

                turn_tiles(0, range(TC))
                scores(0, 0)
                turn_tiles(0, range(TC, NT))
                scores(0, 1)
                ffn(0)
                for c in range(NC):
                    turn_tiles(1, range(TC * c, TC * (c + 1)))
                    pe.wait_ge(ntl_ready, NT + TC * (c + 1))
                    passes(mxp[:, c * BANK:(c + 1) * BANK], (wlat_h, wlat_l), nt, NK, lambda w, k: w[:, k, :],
                           lambda t, k: t[:, k, c * BANK:(c + 1) * BANK]).then_inc(lat_done, 1)
                for e in sched:
                    if e[0] == "Q":
                        g, c = e[1:]
                        n = q_order.index((g, c))
                        if n < 2:
                            pe.wait_ge(gelu_ready, NT)
                        else:
                            pe.wait_ge(q_ready, n - 1)
                        passes(prod[n % 2], (w2_h, w2_l), nt, NK, lambda w, k: w[:, k, P * g:P * (g + 1)],
                               lambda t, k: t[:, k, c * BANK:(c + 1) * BANK]).then_inc(q_done, 1)
                    elif e[0] == "V":
                        i = e[1]
                        if i < 2:
                            pe.wait_ge(scol_ready, 1)
                        else:
                            pe.wait_ge(v_ready, i - 1)
                        pe.wait_ge(latl_ready, NC)
                        passes(vbank[i % 2][:], (lat_h, lat_l), (wkv_h, wkv_l), 1, lambda t, k: t[L:P, P * i:P * (i + 1)],
                               lambda w, k: w[L:P, :]).then_inc(v_done, 1)
                    elif e[0] == "K":
                        g, c = e[1:]
                        if m_index[e] == 1:
                            pe.wait_ge(latl_ready, NC)
                        else:
                            pe.wait_ge(m_free, m_index[e] - 1)
                        passes(mxp[:, 0:BANK], (wkv_h, wkv_l), (lat_h, lat_l), 1, lambda w, k: w[0:L, P * g:P * (g + 1)],
                               lambda t, k: t[0:L, c * BANK:(c + 1) * BANK]).then_inc(m_done, 1)
                    elif e[0] == "MX":
                        g, i, heads = e[1:]
                        pe.wait_ge(m_free, m_index[e] - 1)
                        tc = i // TC
                        if (i % TC, heads[0]) == (0, 0):
                            pe.wait_ge(k_stack, STACK * NC * (g + 1))
                            pe.wait_ge(q_stack, STACK * order_of(g, tc))
                        for n, h in enumerate(heads):
                            lhs = qs[0:ROWS, g % 2, tc, h, P * (i % TC):P * (i % TC + 1)]
                            keys = P * (i + 1)
                            for c in range(NC):
                                w = min(BANK, keys - BANK * c)
                                if w <= 0:
                                    continue
                                own = BANK * (n + c)
                                ends = keys == BANK * c + w
                                pe.matmul(mxp[:, own:own + w], lhs, ks[0:ROWS, g % 2, c, h, 0:w],
                                          start=True, stop=not ends, skip_group_check=True)
                                if ends:
                                    m = pe.matmul(mxp[:, own + w - P:own + w], ident_b[:], mask_b[:], start=False, stop=True,
                                                  skip_group_check=True)
                        m.then_inc(m_done, 1)
                    elif e[0] == "XT":
                        g, c = e[1:]
                        pe.wait_ge(m_free, m_index[e] - 1)
                        pe.transpose(mxp[0:HQ * TC, 0:P], mx[:, c, :, :].rearrange("p h i -> p (h i)"), ident[:]
                                     ).then_inc(m_done, 1)
                    elif e[0] == "S":
                        u = e[1]
                        g, c, jp, h = uses[u]
                        if u == 0:
                            pe.wait_ge(ntl_ready, 2 * NT)
                        elif u == 1:
                            pe.wait_ge(q_ready, NQ * NC)
                        else:
                            pe.wait_ge(exp_ready, u - 1)
                        if (jp, h) == (0, 0):
                            pe.wait_ge(m_stack, 16 * order_of(g, c))
                        for n in range(2):
                            j = 2 * jp + n
                            w = width(c, j)
                            own = BANK - w if n == 0 else BANK
                            m = pe.matmul(score[u % 2][:, own:own + w], ks[0:ROWS + 1, g % 2, j // TC, h, P * (j % TC):P * (j % TC + 1)],
                                          qs[0:ROWS + 1, g % 2, c, h, BANK - w:BANK], start=True, stop=True)
                        m.then_inc(s_done, 1)
                    elif e[0] == "PV":
                        q = e[1]
                        g, c, jp = steps[q]
                        pe.wait_ge(exp_ready, HQ * (q + 1))
                        pe.wait_ge(mask_ready, masks_upto[HQ * (q + 1)])
                        if q == 0:
                            pe.wait_ge(v_ready, NT)
                        if jp == 0 and order_of(g, c) > 1:
                            pe.wait_ge(bank_free, order_of(g, c) - 1)
                        w0 = width(c, 2 * jp)
                        for n in range(2):
                            j = 2 * jp + n
                            w = width(c, j)
                            for h in range(HQ):
                                slot = (HQ * q + h) % SLOTS
                                m = pe.matmul(acc[h * DH:(h + 1) * DH, BANK - w:BANK],
                                              v_sb[:, j, P * g + DH * h:P * g + DH * (h + 1)],
                                              pr[:, slot, n * w0:n * w0 + w], start=(j == 0), stop=(j == TC * (c + 1) - 1),
                                              skip_group_check=True)
                        m.then_inc(pv_done, 1)
                    elif e[0] == "DEN":
                        q = e[1]
                        g, c, jp = steps[q]
                        pe.wait_ge(sum_ready, sums_upto[HQ * (q + 1)])
                        w0 = width(c, 2 * jp)
                        for h in range(HQ):
                            m = pe.matmul(den[h * DH:(h + 1) * DH, BANK - w0:BANK], ones[:], dsum[:, h, 0:w0],
                                          start=(jp == 0), stop=(jp == 2 * c + 1), skip_group_check=True)
                        m.then_inc(den_done, 1)
                pe.wait_ge(w2_in, 32)
                pe.wait_ge(exp_ready, USES * NQ)
                for i in range(NT):
                    pe.wait_ge(ol_ready, NQ * (i // TC + 1))
                    if i >= 2:
                        pe.wait_ge(x1_ready, NT + i - 1)
                    passes(prod[i % 2], nt, (w2_h, w2_l), NK, lambda t, k: t[:, k, P * i:P * (i + 1)],
                           lambda w, k: w[:, k, :]).then_inc(o_done, 1)
                turn_tiles(2, range(TC))
                scores(1, 0)
                turn_tiles(2, range(TC, NT))
                scores(1, 1)
                ffn(1)
                end_of_sequence(pe)

        @block.vector
        def _(dve):
            nc.vector.memset(ks[ROWS:ROWS + 1].rearrange("p b c h t -> p (b c h t)").bitcast(F32), -1.0).then_inc(consts, 1)
            for n, ((high, raw), low) in enumerate(zip(weight_parts_h, weight_parts_l)):
                dve.wait_ge(split, 2 * n + 1)
                nc.vector.tensor_tensor(low, raw, high.bitcast(F32), ALU.subtract).then_inc(split, 1)
            dve.wait_ge(consts, CONSTS)

            with dve.Fori(0, B):
                count = [0]

                def step(ins):
                    count[0] += 1
                    ins.then_inc(dve_step, 1)

                def settled():
                    dve.wait_ge(dve_step, count[0])

                def statistics(s, c):
                    tiles = range(TC * c, TC * (c + 1))
                    k = slice(TC * c, TC * (c + 1))
                    if s == 0:
                        dve.wait_ge(x_in[c], 16)
                    else:
                        dve.wait_ge(x1_ready, NT * (s - 1) + TC * (c + 1))
                    for i in tiles:
                        step(nc.vector.bn_stats(stats[:, i, :], (xin if s == 0 else x1)[:, i, :]))
                    settled()
                    for i in tiles:
                        step(nc.vector.bn_aggr(mv[:, i, :], stats[:, i, :]))
                    settled()
                    nc.vector.tensor_scalar(var[:, k], mv[:, k, 1], EPS, None, ALU.add).then_inc(var_ready, 1)
                    dve.wait_ge(rstd_ready, NC * s + c + 1)
                    nc.vector.scalar_tensor_tensor(out=nmr[:, k], in0=mv[:, k, 0], scalar=-1.0, in1=rstd[:, k],
                                                   op0=ALU.mult, op1=ALU.mult).then_inc(nmr_ready, 1)

                def turned_low(s, tiles):
                    for i in tiles:
                        dve.wait_ge(nth_ready, NT * s + i + 1)
                        cols = slice(P * i, P * (i + 1))
                        nc.vector.tensor_tensor(nt_l[:, :, cols], turned[i % 2].rearrange("p (k t) -> p k t", k=NK),
                                                nt_h[:, :, cols].bitcast(F32), ALU.subtract).then_inc(ntl_ready, 1)

                def route(f):
                    dve.wait_ge(scol_done, f + 1)
                    nc.vector.tensor_copy(scol[:], acc[:, 0:NT]).then_inc(scol_ready, 1)
                    dve.wait_ge(scol_ready, f + 1)
                    dve.wait_ge(srow_ready, NC * (f + 1))
                    for i in range(NT):
                        step(nc.vector.tensor_scalar(junk[:], srow[:], scol[:, i:i + 1], 0.0, ALU.is_gt, ALU.add,
                                                     accum_out=n_gt[:, i:i + 1]))
                        settled()
                        upto = P * (i + 1)
                        step(nc.vector.scalar_tensor_tensor(out=junk[:, 0:upto], in0=srow[:, 0:upto],
                                                            scalar=scol[:, i:i + 1], in1=earlier[:, T - upto:T],
                                                            op0=ALU.is_equal, op1=ALU.mult,
                                                            accum_out=n_eq[:, i:i + 1]))
                        settled()
                    step(nc.vector.tensor_tensor(sel[:], n_gt[:], n_eq[:], ALU.add))
                    settled()
                    step(nc.vector.tensor_scalar(rest[:], sel[:], float(KEEP), 0.5, ALU.is_ge, ALU.mult))
                    settled()
                    step(nc.vector.tensor_scalar(sel[:], rest[:], -1.0, 0.5, ALU.mult, ALU.add))
                    step(nc.vector.tensor_tensor(gain[:], rest[:], rstd[:], ALU.mult))
                    step(nc.vector.tensor_tensor(shift[:], rest[:], nmr[:], ALU.mult))
                    settled()
                    step(nc.vector.tensor_scalar(gain[:], gain[:], 1.0, None, ALU.add))
                    settled()
                    for i in range(NT):
                        step(nc.vector.tensor_scalar(x1[:, i, :], (x1 if f else xin)[:, i, :], gain[:, i:i + 1],
                                                     shift[:, i:i + 1], ALU.mult, ALU.add))
                    settled()

                def combine(f, tiles):
                    for i in tiles:
                        dve.wait_ge(gelu_ready, NT * f + i + 1)
                        nc.vector.scalar_tensor_tensor(out=x1[:, i, :], in0=act_out[:, i, :], scalar=sel[:, i:i + 1],
                                                       in1=x1[:, i, :], op0=ALU.mult, op1=ALU.add).then_inc(x1_ready, 1)

                halves = (range(TC), range(TC, NT))
                statistics(0, 0)
                statistics(0, 1)
                turned_low(0, range(NT))
                route(0)
                for c in range(NC):
                    combine(0, halves[c])
                    statistics(1, c)
                for c in range(NC):
                    turned_low(1, halves[c])
                    cols = slice(c * BANK, (c + 1) * BANK)
                    dve.wait_ge(lath_ready, c + 1)
                    nc.vector.tensor_tensor(lat_l[:, cols], mxp[:, cols], lat_h[:, cols].bitcast(F32), ALU.subtract
                                            ).then_inc(latl_ready, 1)
                for e in sched:
                    if e[0] == "V":
                        i = e[1]
                        dve.wait_ge(v_done, i + 1)
                        nc.vector.tensor_copy(v_sb[:, i, :], vbank[i % 2][:]).then_inc(v_ready, 1)
                    elif e[0] == "K":
                        dve.wait_ge(kh_ready, order_of(*e[1:]))
                        nc.vector.tensor_tensor(kst_l[:], mxp[:, 0:BANK], kst_h[:].bitcast(F32), ALU.subtract
                                                ).then_inc(m_free, 1)
                    elif e[0] == "MX":
                        g, i, heads = e[1:]
                        c, keys = i // TC, P * (i + 1)
                        dve.wait_ge(m_done, m_index[e])
                        if len(heads) == 2:
                            nc.vector.tensor_reduce(mx[:, c, heads[0]:heads[1] + 1, i % TC],
                                                    mxp[:].rearrange("p (h s) -> p h s", h=2)[:, :, 0:keys],
                                                    AX_X, ALU.max).then_inc(m_free, 1)
                        else:
                            nc.vector.tensor_reduce(mx[:, c, heads[0], i % TC:i % TC + 1], mxp[:, 0:keys],
                                                    AX_X, ALU.max).then_inc(m_free, 1)
                    elif e[0] == "XT":
                        g, c = e[1:]
                        dve.wait_ge(m_done, m_index[e])
                        if order_of(g, c) > 1:
                            dve.wait_ge(m_stack, 16 * (order_of(g, c) - 1))
                        nc.vector.tensor_copy(mxt[:], mxp[0:HQ * TC, 0:P]).then_inc(m_free, 1)
                    elif e[0] == "DEN":
                        q = e[1]
                        g, c, jp = steps[q]
                        if jp < 2 * c + 1:
                            continue
                        heads = ht[:, g, c * BANK:(c + 1) * BANK]
                        dve.wait_ge(ql_ready, order_of(g, c))
                        dve.wait_ge(pv_done, q + 1)
                        step(nc.vector.tensor_copy(acc_sb[:], acc[:]))
                        dve.wait_ge(den_done, q + 1)
                        nc.vector.tensor_copy(heads, den[:]).then_inc(bank_free, 1)
                        dve.wait_ge(bank_free, order_of(g, c))
                        step(nc.vector.reciprocal(heads, heads))
                        settled()
                        nc.vector.tensor_tensor(heads, acc_sb[:], heads, ALU.mult).then_inc(heads_ready, 1)
                        dve.wait_ge(heads_ready, order_of(g, c))
                for c in range(NC):
                    cols = slice(c * BANK, (c + 1) * BANK)
                    for g in range(NQ):
                        dve.wait_ge(oh_ready, NQ * c + g + 1)
                        nc.vector.tensor_tensor(nt_l[:, g, cols], ht[:, g, cols], nt_h[:, g, cols].bitcast(F32),
                                                ALU.subtract).then_inc(ol_ready, 1)
                for c in range(NC):
                    for i in halves[c]:
                        dve.wait_ge(o_done, i + 1)
                        nc.vector.tensor_tensor(x1[:, i, :], prod[i % 2], x1[:, i, :], ALU.add).then_inc(x1_ready, 1)
                    statistics(2, c)
                turned_low(2, range(NT))
                route(1)
                combine(1, range(NT))
                end_of_sequence(dve)


def kernel(**inputs):
    import numpy as np
    import concourse.bacc as bacc
    from concourse.bass_utils import run_bass_kernel_spmd

    x = np.ascontiguousarray(inputs["L0_attn_hidden_states"])
    q_to_latent, v_up = np.asarray(inputs["L0_attn_q_to_latent"]), np.asarray(inputs["L0_attn_v_up"])
    latent, width = q_to_latent.shape[2], q_to_latent.shape[1]

    def interleaved(w):
        return w.reshape(w.shape[0], -1, P // width, width).transpose(0, 1, 3, 2).reshape(w.shape)

    arrays = {
        "x": x,
        "w_q": interleaved(np.asarray(inputs["L0_attn_Wq"]).T),
        "w_lat": np.concatenate([np.asarray(inputs["L0_attn_Wk_down"]), np.asarray(inputs["L0_attn_Wv_down"])]).T,
        "w_qk": interleaved(q_to_latent.transpose(2, 0, 1).reshape(latent, -1)),
        "w_vu": v_up.transpose(1, 0, 2).reshape(latent, -1),
        "w_out": np.asarray(inputs["L0_attn_Wout"]).T,
        "w_router": np.asarray(inputs["L0_ffn_w_router"]),
        "w_block": np.asarray(inputs["L0_ffn_w_block"]),
    }
    arrays = {name: np.ascontiguousarray(a) for name, a in arrays.items()}
    nc = bacc.Bacc("TRN2", target_bir_lowering=False, num_devices=1)
    aps = {name: nc.dram_tensor(f"{name}_dram", a.shape, F32, kind="ExternalInput").ap() for name, a in arrays.items()}
    e = x.shape[2]
    scratch = [nc.dram_tensor(f"scratch_{n}", (2, P, e // P, e), F32, kind="Internal").ap() for n in "qo"]
    result = nc.dram_tensor("out_dram", x.shape, F32, kind="ExternalOutput").ap()
    macaron(nc, *aps.values(), *scratch, result)
    r = run_bass_kernel_spmd(nc, [{f"{name}_dram": a for name, a in arrays.items()}], core_ids=[0])
    return r.results[0]["out_dram"]
```
